# Optimizing a Trainium2 kernel written in Bass

```python
import numpy as np
import jax
import jax.numpy as jnp

def _softmax(x, axis=-1):
    return jax.nn.softmax(x, axis=axis)

def _gelu(x):
    return jax.nn.gelu(x, approximate=True)

def _silu(x):
    return jax.nn.silu(x)

def _sigmoid(x):
    return jax.nn.sigmoid(x)

def _layernorm(x, axis=-1, eps=1e-05):
    m = jnp.mean(x, axis=axis, keepdims=True)
    v = jnp.var(x, axis=axis, keepdims=True)
    return (x - m) / jnp.sqrt(v + eps)

def _scatter_add(tgt, idx, src, axis=0):
    return tgt.at[idx].add(src)

def _segment_sum(src, seg, n):
    return jax.ops.segment_sum(src, seg, n)
kernel_name = 'mk_decoder_postln_d1_seqx_r4_f1ebf5'

def setup_inputs(seed: int=0):
    np.random.seed(seed)
    _w = jnp.asarray

    def _rec_inputs():
        import jax
        import jax.numpy as jnp
        _rk = jax.random.key(seed)
        x = -0.0002928 + 1 * jax.random.normal(jax.random.fold_in(_rk, 1), (16, 256, 512), jnp.float32)
        _lenS = 256 - jax.random.randint(jax.random.fold_in(_rk, 7), (16,), 0, max(1, 256 // 4) + 1, jnp.int32)
        _lenS2 = 256 - jax.random.randint(jax.random.fold_in(_rk, 8), (16,), 0, max(1, 256 // 4) + 1, jnp.int32)
        _ctx_2048P = jax.random.normal(jax.random.fold_in(_rk, 11), (16, 16, 512), jnp.float32)
        _ctx_2048c = jax.random.dirichlet(jax.random.fold_in(_rk, 511), 0.3 * jnp.ones((16,), jnp.float32), (16, 256))
        _ctx_2048t = jnp.einsum('bsk,bkd->bsd', _ctx_2048c, _ctx_2048P)
        _ctx_2048t = _ctx_2048t * jax.lax.rsqrt(jnp.mean(jnp.square(_ctx_2048t)) + 1e-12) * 0.953939
        ctx_2048 = -1.39393e-06 + 0.999914 * (_ctx_2048t + 0.3 * jax.random.normal(jax.random.fold_in(_rk, 611), (16, 256, 512), jnp.float32))
        return (x, ctx_2048)
    x, ctx_2048 = _rec_inputs()

    def _L0_attn_setup():
        import jax, jax.numpy as jnp
        import numpy as np
        HIDDEN = 512
        N_HEADS = 16
        N_KV_HEADS = 4
        HEAD_DIM = HIDDEN // N_HEADS
        ROPE_THETA = 10000.0
        B, S = (1, 512)

        def _apply_rope(x, position_ids, theta=ROPE_THETA):
            b, s, h, hd = x.shape
            dim_half = hd // 2
            inv_freq = 1.0 / theta ** (jnp.arange(0, dim_half, 2, dtype=jnp.float32) / dim_half)
            freqs = position_ids[:, :, None].astype(jnp.float32) * inv_freq[None, None, :]
            cos = jnp.cos(freqs)[:, :, None, :]
            sin = jnp.sin(freqs)[:, :, None, :]
            x_rot = x[..., :dim_half].reshape(b, s, h, dim_half // 2, 2)
            x0, x1 = (x_rot[..., 0], x_rot[..., 1])
            rotated = jnp.stack([x0 * cos - x1 * sin, x0 * sin + x1 * cos], axis=-1)
            rotated = rotated.reshape(b, s, h, dim_half)
            return jnp.concatenate([rotated, x[..., dim_half:]], axis=-1)
        key = jax.random.key(seed)
        k0, k1, k2, k3, k4 = jax.random.split(key, 5)
        std = 0.02
        return {'hidden_states': jax.random.normal(k0, (B, S, HIDDEN), dtype=jnp.float32), 'Wq': jax.random.normal(k1, (HIDDEN, N_HEADS * HEAD_DIM), dtype=jnp.float32) * std, 'Wk': jax.random.normal(k2, (HIDDEN, N_KV_HEADS * HEAD_DIM), dtype=jnp.float32) * std, 'Wv': jax.random.normal(k3, (HIDDEN, N_KV_HEADS * HEAD_DIM), dtype=jnp.float32) * std, 'Wo': jax.random.normal(k4, (HIDDEN, HIDDEN), dtype=jnp.float32) * std}
    _L0_attn_all = _L0_attn_setup()
    _L0_attn_in = {k: v for k, v in _L0_attn_all.items() if k in ('Wq', 'Wk', 'Wv', 'Wo')}
    del _L0_attn_all

    def _L0_xattn_setup():
        import jax, jax.numpy as jnp
        import numpy as np
        B, S, E, NH = (2, 256, 512, 16)
        DH = E // NH
        EPS = 1e-06

        def _mlstm_forward(q, k, v, Wi, bi, Wf, bf, ln_scale):
            b, s, e = q.shape
            nh = Wi.shape[1]
            dh = e // nh
            x = jnp.concatenate([q, k, v], axis=-1)
            ig = (x @ Wi + bi).transpose(0, 2, 1)[..., None]
            fg = (x @ Wf + bf).transpose(0, 2, 1)[..., None]
            split = lambda t: t.reshape(b, s, nh, dh).transpose(0, 2, 1, 3)
            qh, kh, vh = (split(q), split(k), split(v))
            log_f = jax.nn.log_sigmoid(fg)
            log_f_cum = jnp.concatenate([jnp.zeros((b, nh, 1, 1), q.dtype), jnp.cumsum(log_f, axis=2)], axis=2)
            fg_mat = log_f_cum - jnp.transpose(log_f_cum, (0, 1, 3, 2))
            ltr = jnp.tril(jnp.ones((s, s), dtype=bool))
            log_fg = jnp.where(ltr, fg_mat[:, :, 1:, 1:], -jnp.inf)
            log_D = log_fg + jnp.transpose(ig, (0, 1, 3, 2))
            max_log_D = jnp.max(log_D, axis=-1, keepdims=True)
            D = jnp.exp(log_D - max_log_D)
            qk = jnp.einsum('bhsd,bhtd->bhst', qh, kh) / jnp.sqrt(jnp.asarray(dh, q.dtype))
            C = qk * D
            normalizer = jnp.maximum(jnp.abs(C.sum(-1, keepdims=True)), jnp.exp(-max_log_D))
            Cn = C / (normalizer + EPS)
            h = jnp.einsum('bhst,bhtd->bhsd', Cn, vh)
            mu = h.mean(-1, keepdims=True)
            var = ((h - mu) ** 2).mean(-1, keepdims=True)
            hn = (h - mu) * jax.lax.rsqrt(var + EPS)
            hn = hn * ln_scale.reshape(1, nh, 1, dh)
            return hn.transpose(0, 2, 1, 3).reshape(b, s, e)
        key = jax.random.key(seed)
        ks = jax.random.split(key, 6)
        q = jax.random.normal(ks[0], (B, S, E), dtype=jnp.float32)
        k = jax.random.normal(ks[1], (B, S, E), dtype=jnp.float32)
        v = jax.random.normal(ks[2], (B, S, E), dtype=jnp.float32)
        Wi = jax.random.normal(ks[3], (3 * E, NH), dtype=jnp.float32) * 0.02
        bi = jax.random.normal(ks[4], (NH,), dtype=jnp.float32) * 0.1
        Wf = jax.random.normal(ks[5], (3 * E, NH), dtype=jnp.float32) * 0.02
        bf = jnp.linspace(3.0, 6.0, NH, dtype=jnp.float32)
        ln_scale = jnp.ones((E,), dtype=jnp.float32)
        return {'q': q, 'k': k, 'v': v, 'Wi': Wi, 'bi': bi, 'Wf': Wf, 'bf': bf, 'ln_scale': ln_scale}
    _L0_xattn_all = _L0_xattn_setup()
    _L0_xattn_in = {k: v for k, v in _L0_xattn_all.items() if k in ('Wi', 'bi', 'Wf', 'bf', 'ln_scale')}
    del _L0_xattn_all

    def _L0_ffn_setup():
        import jax, jax.numpy as jnp
        import numpy as np
        DIM = 512
        EXPERT_DIM = 256
        N_EXPERTS = 16
        TOPK = 2
        N_SHARED = 1
        B, T = (4, 512)
        key = jax.random.key(seed)
        ks = jax.random.split(key, 9)
        s = 0.02
        return {'x': jax.random.normal(ks[0], (B, T, DIM), jnp.float32), 'router_w': jax.random.normal(ks[1], (N_EXPERTS, DIM), jnp.float32) * s, 'router_bias': jnp.zeros((N_EXPERTS,), jnp.float32), 'Wu': jax.random.normal(ks[2], (N_EXPERTS, DIM, EXPERT_DIM), jnp.float32) * s, 'Wg': jax.random.normal(ks[3], (N_EXPERTS, DIM, EXPERT_DIM), jnp.float32) * s, 'Wd': jax.random.normal(ks[4], (N_EXPERTS, EXPERT_DIM, DIM), jnp.float32) * s, 'Su': jax.random.normal(ks[5], (N_SHARED, DIM, EXPERT_DIM * TOPK), jnp.float32) * s, 'Sg': jax.random.normal(ks[6], (N_SHARED, DIM, EXPERT_DIM * TOPK), jnp.float32) * s, 'Sd': jax.random.normal(ks[7], (N_SHARED, EXPERT_DIM * TOPK, DIM), jnp.float32) * s}
    _L0_ffn_all = _L0_ffn_setup()
    _L0_ffn_in = {k: v for k, v in _L0_ffn_all.items() if k in ('router_w', 'router_bias', 'Wu', 'Wg', 'Wd', 'Su', 'Sg', 'Sd')}
    del _L0_ffn_all
    return {'x': x, 'ctx_2048': ctx_2048, 'L0_attn_Wq': _L0_attn_in['Wq'], 'L0_attn_Wk': _L0_attn_in['Wk'], 'L0_attn_Wv': _L0_attn_in['Wv'], 'L0_attn_Wo': _L0_attn_in['Wo'], 'L0_xattn_Wi': _L0_xattn_in['Wi'], 'L0_xattn_bi': _L0_xattn_in['bi'], 'L0_xattn_Wf': _L0_xattn_in['Wf'], 'L0_xattn_bf': _L0_xattn_in['bf'], 'L0_xattn_ln_scale': _L0_xattn_in['ln_scale'], 'L0_ffn_router_w': _L0_ffn_in['router_w'], 'L0_ffn_router_bias': _L0_ffn_in['router_bias'], 'L0_ffn_Wu': _L0_ffn_in['Wu'], 'L0_ffn_Wg': _L0_ffn_in['Wg'], 'L0_ffn_Wd': _L0_ffn_in['Wd'], 'L0_ffn_Su': _L0_ffn_in['Su'], 'L0_ffn_Sg': _L0_ffn_in['Sg'], 'L0_ffn_Sd': _L0_ffn_in['Sd']}

def reference(x, ctx_2048, L0_attn_Wq, L0_attn_Wk, L0_attn_Wv, L0_attn_Wo, L0_xattn_Wi, L0_xattn_bi, L0_xattn_Wf, L0_xattn_bf, L0_xattn_ln_scale, L0_ffn_router_w, L0_ffn_router_bias, L0_ffn_Wu, L0_ffn_Wg, L0_ffn_Wd, L0_ffn_Su, L0_ffn_Sg, L0_ffn_Sd):
    import jax
    import jax.numpy as jnp

    def _L0_attn_ref(hidden_states, Wq, Wk, Wv, Wo):
        import jax, jax.numpy as jnp
        import numpy as np
        HIDDEN = 512
        N_HEADS = 16
        N_KV_HEADS = 4
        HEAD_DIM = HIDDEN // N_HEADS
        ROPE_THETA = 10000.0
        B, S = (1, 512)

        def _apply_rope(x, position_ids, theta=ROPE_THETA):
            b, s, h, hd = x.shape
            dim_half = hd // 2
            inv_freq = 1.0 / theta ** (jnp.arange(0, dim_half, 2, dtype=jnp.float32) / dim_half)
            freqs = position_ids[:, :, None].astype(jnp.float32) * inv_freq[None, None, :]
            cos = jnp.cos(freqs)[:, :, None, :]
            sin = jnp.sin(freqs)[:, :, None, :]
            x_rot = x[..., :dim_half].reshape(b, s, h, dim_half // 2, 2)
            x0, x1 = (x_rot[..., 0], x_rot[..., 1])
            rotated = jnp.stack([x0 * cos - x1 * sin, x0 * sin + x1 * cos], axis=-1)
            rotated = rotated.reshape(b, s, h, dim_half)
            return jnp.concatenate([rotated, x[..., dim_half:]], axis=-1)
        b, s, _ = hidden_states.shape
        groups = N_HEADS // N_KV_HEADS
        q = (hidden_states @ Wq).reshape(b, s, N_HEADS, HEAD_DIM)
        k = (hidden_states @ Wk).reshape(b, s, N_KV_HEADS, HEAD_DIM)
        v = (hidden_states @ Wv).reshape(b, s, N_KV_HEADS, HEAD_DIM)
        position_ids = jnp.broadcast_to(jnp.arange(s)[None, :], (b, s))
        q = _apply_rope(q, position_ids)
        k = _apply_rope(k, position_ids)
        if groups > 1:
            k = jnp.repeat(k, groups, axis=2)
            v = jnp.repeat(v, groups, axis=2)
        scale = 1.0 / jnp.sqrt(jnp.float32(HEAD_DIM))
        scores = jnp.einsum('bshd,bthd->bhst', q, k) * scale
        attn = jax.nn.softmax(scores, axis=-1)
        out = jnp.einsum('bhst,bthd->bshd', attn, v)
        out = out.reshape(b, s, HIDDEN)
        return out @ Wo

    def _L0_xattn_ref(q, k, v, Wi, bi, Wf, bf, ln_scale):
        import jax, jax.numpy as jnp
        import numpy as np
        B, S, E, NH = (2, 256, 512, 16)
        DH = E // NH
        EPS = 1e-06

        def _mlstm_forward(q, k, v, Wi, bi, Wf, bf, ln_scale):
            b, s, e = q.shape
            nh = Wi.shape[1]
            dh = e // nh
            x = jnp.concatenate([q, k, v], axis=-1)
            ig = (x @ Wi + bi).transpose(0, 2, 1)[..., None]
            fg = (x @ Wf + bf).transpose(0, 2, 1)[..., None]
            split = lambda t: t.reshape(b, s, nh, dh).transpose(0, 2, 1, 3)
            qh, kh, vh = (split(q), split(k), split(v))
            log_f = jax.nn.log_sigmoid(fg)
            log_f_cum = jnp.concatenate([jnp.zeros((b, nh, 1, 1), q.dtype), jnp.cumsum(log_f, axis=2)], axis=2)
            fg_mat = log_f_cum - jnp.transpose(log_f_cum, (0, 1, 3, 2))
            ltr = jnp.tril(jnp.ones((s, s), dtype=bool))
            log_fg = jnp.where(ltr, fg_mat[:, :, 1:, 1:], -jnp.inf)
            log_D = log_fg + jnp.transpose(ig, (0, 1, 3, 2))
            max_log_D = jnp.max(log_D, axis=-1, keepdims=True)
            D = jnp.exp(log_D - max_log_D)
            qk = jnp.einsum('bhsd,bhtd->bhst', qh, kh) / jnp.sqrt(jnp.asarray(dh, q.dtype))
            C = qk * D
            normalizer = jnp.maximum(jnp.abs(C.sum(-1, keepdims=True)), jnp.exp(-max_log_D))
            Cn = C / (normalizer + EPS)
            h = jnp.einsum('bhst,bhtd->bhsd', Cn, vh)
            mu = h.mean(-1, keepdims=True)
            var = ((h - mu) ** 2).mean(-1, keepdims=True)
            hn = (h - mu) * jax.lax.rsqrt(var + EPS)
            hn = hn * ln_scale.reshape(1, nh, 1, dh)
            return hn.transpose(0, 2, 1, 3).reshape(b, s, e)
        return _mlstm_forward(q, k, v, Wi, bi, Wf, bf, ln_scale)

    def _L0_ffn_ref(x, router_w, router_bias, Wu, Wg, Wd, Su, Sg, Sd):
        import jax, jax.numpy as jnp
        import numpy as np
        DIM = 512
        EXPERT_DIM = 256
        N_EXPERTS = 16
        TOPK = 2
        N_SHARED = 1
        B, T = (4, 512)
        Bx, Tx, D = x.shape
        flat = x.reshape(Bx * Tx, D)
        logits = flat @ router_w.T
        scores = jax.nn.softmax(logits, axis=-1)
        _, topk_idx = jax.lax.top_k(logits + router_bias, TOPK)
        topk_scores = jnp.take_along_axis(scores, topk_idx, axis=-1)
        topk_scores = topk_scores / topk_scores.sum(-1, keepdims=True)
        combine = jnp.einsum('nk,nke->ne', topk_scores, jax.nn.one_hot(topk_idx, N_EXPERTS, dtype=scores.dtype))
        out = jnp.zeros_like(flat)
        for e in range(N_EXPERTS):
            h = jax.nn.silu(flat @ Wu[e]) * (flat @ Wg[e])
            out = out + combine[:, e:e + 1] * (h @ Wd[e])
        for s in range(N_SHARED):
            out = out + jax.nn.silu(flat @ Su[s]) * (flat @ Sg[s]) @ Sd[s]
        return out.reshape(Bx, Tx, D)
    x = _layernorm(x + _L0_attn_ref(x, L0_attn_Wq, L0_attn_Wk, L0_attn_Wv, L0_attn_Wo), axis=-1)
    x = _layernorm(x + _L0_xattn_ref(x, ctx_2048, ctx_2048, L0_xattn_Wi, L0_xattn_bi, L0_xattn_Wf, L0_xattn_bf, L0_xattn_ln_scale), axis=-1)
    x = _layernorm(x + _L0_ffn_ref(x, L0_ffn_router_w, L0_ffn_router_bias, L0_ffn_Wu, L0_ffn_Wg, L0_ffn_Wd, L0_ffn_Su, L0_ffn_Sg, L0_ffn_Sd), axis=-1)
    return x

_drawn_inputs = setup_inputs


def setup_inputs(seed=0):
    import zlib

    import numpy as np

    out = dict(_drawn_inputs(seed))
    spreads = {'L0_xattn_ln_scale': (1.0, 0.2), 'L0_ffn_router_bias': (0.0, 2.0)}
    factors = {'L0_attn_Wq': 8.0,
     'L0_attn_Wk': 8.0,
     'L0_attn_Wv': 3.832,
     'L0_attn_Wo': 3.725,
     'L0_xattn_bi': 64.0,
     'L0_ffn_router_w': 3.074}
    for name, (base, spread) in spreads.items():
        noise = np.random.default_rng([zlib.crc32(name.encode()), seed]).standard_normal(out[name].shape)
        drawn = base * np.exp(spread * noise) if base else spread * noise
        out[name] = jnp.asarray(drawn.astype(out[name].dtype))
    for name, factor in factors.items():
        out[name] = (out[name] * factor).astype(out[name].dtype)
    return out
```

```python
import math
from contextlib import ExitStack

import numpy as np

import concourse.bass as bass
from concourse import mybir

F32 = mybir.dt.float32
F32R = mybir.dt.float32r
I32 = mybir.dt.int32
U32 = mybir.dt.uint32
ALU = mybir.AluOpType
ACT = mybir.ActivationFunctionType
AX = mybir.AxisListType

P = 128
B, S, D = 16, 256, 512
ST = S // P
KC = D // P
H, HD, KV = 16, 32, 4
GQ = H // KV
QKV = D + 2 * KV * HD
QKH = H + KV
ROT = HD // 2
PAIRS = H // 2
HALF = H // 2
VA = HD + 1
E, TOPK, F = 16, 2, 256
FC = F // P
SF = TOPK * F
SC = SF // P
N = B * S
NT = N // P
MT = (N * TOPK + E * (P - 1)) // P
MT += -MT % 4
FILL = MT // 5
SCALE = 1.0 / math.sqrt(HD)
LN_EPS = 1e-5
ML_EPS = 1e-6
MASKED = -float(2 ** 100)


class Signal:

    def __init__(self, sem, per):
        self.sem, self.per = sem, per

    def at(self, b, n):
        return b * self.per + n


def wait(eng, signal, b, n, rest=None):
    value = signal.at(b, n)
    if isinstance(value, int) and value == 0:
        return
    if rest is not None and not isinstance(value, int):
        register, met = rest
        eng.reg_mov(register, value)
        eng.wait_ge(met, 1)
        value = register
    eng.wait_ge(signal.sem, value)


class Steps:

    def __init__(self, eng, done, b):
        self.eng, self.done, self.b, self.n = eng, done, b, 0

    def __call__(self, ins, rest=None):
        ins.then_inc(self.done.sem, 1)
        self.n += 1
        wait(self.eng, self.done, self.b, self.n, rest)

    def end(self):
        assert self.n == self.done.per, (self.n, self.done.per)


def bcast(ap, shape):
    return ap.unsqueeze(len(ap.shape)).to_broadcast(shape)


def decoder_layer(nc, x, xT, ctx_in, ctxT, wqkv, wo, gate_w, gate_b, ln_scale, router_w, router_b,
                  expert_ug, expert_d, su, sg, sd,
                  rope_cos, rope_sin, ident, mask, before, iota, out):
    x2_dram = nc.dram_tensor("x2_rows", [N, D], F32).ap()
    base_dram = nc.dram_tensor("base_rows", [N, D], F32).ap()
    xs_dram = nc.dram_tensor("sorted_rows", [MT * P, D], F32).ap()
    ys_dram = nc.dram_tensor("expert_rows", [MT * P, D], F32).ap()
    with ExitStack() as keep:
        logits = keep.enter_context(nc.sbuf_tensor("logits", [P, NT, E], F32))
        choice = keep.enter_context(nc.sbuf_tensor("choice", [P, NT, TOPK], F32))
        share = keep.enter_context(nc.sbuf_tensor("share", [P, TOPK, NT], F32))
        pos_i = keep.enter_context(nc.sbuf_tensor("pos_i", [P, TOPK, NT], I32))
        attention_and_mlstm(nc, x, xT, ctx_in, ctxT, wqkv, wo, gate_w, gate_b, ln_scale, router_w, router_b,
                            su, sg, sd, rope_cos, rope_sin, ident, mask,
                            x2_dram, base_dram, xs_dram, logits, choice)
        experts(nc, expert_ug, expert_d, ident, before, iota,
                x2_dram, xs_dram, ys_dram, logits, choice, share, pos_i)
        combine(nc, base_dram, ys_dram, share, pos_i, out)


def attention_and_mlstm(nc, x, xT, ctx_in, ctxT, wqkv, wo, gate_w, gate_b, ln_scale, router_w, router_b,
                        su, sg, sd, rope_cos, rope_sin, ident, mask,
                        x2_dram, base_dram, xs_dram, logits, choice):
    with ExitStack() as ctx:
        def sb(name, shape, dt=F32):
            return ctx.enter_context(nc.sbuf_tensor(name, shape, dt))

        def sig(name, per):
            return Signal(ctx.enter_context(nc.semaphore(name)), per)

        wqkv_sb = sb("wqkv_sb", [P, KC, QKV])
        wo_sb = sb("wo_sb", [P, KC, D])
        su_sb = sb("su_sb", [P, KC, SF])
        sg_sb = sb("sg_sb", [P, KC, SF])
        sd_sb = sb("sd_sb", [P, SC, D])
        rw_sb = sb("rw_sb", [P, KC, E])
        rb_sb = sb("rb_sb", [P, E])
        lns_sb = sb("lns_sb", [P, D])
        cos_sb = sb("cos_sb", [P, ST, ROT])
        sin_sb = sb("sin_sb", [P, ST, 2, ROT // 2])
        id_sb = sb("id_sb", [P, P])
        idr_sb = sb("idr_sb", [P, P], F32R)
        mask_sb = sb("mask_sb", [P, P])
        maskr_sb = sb("maskr_sb", [P, P], F32R)
        gb_sb = sb("gb_sb", [48, 1])
        gw_raw = sb("gw_raw", [P, 3 * KC, 2, H])
        gw_hi = sb("gw_hi", [P, 2 * KC, P], F32R)
        gw_lo = sb("gw_lo", [P, 2 * KC, P], F32R)
        ones_row = sb("ones_row", [H, S])
        eps_half = sb("eps_half", [P, 2 * H])

        xT_sb = sb("xT_sb", [P, KC, S])
        x_sb = sb("x_sb", [P, ST, D])
        qk_sb = sb("qk_sb", [P, ST, QKH, HD])
        rope_a = sb("rope_a", [P, QKH, ROT])
        rope_b = sb("rope_b", [P, QKH, ROT // 2, 2])
        v_sb = sb("v_sb", [P, ST, KV, VA])
        qkT_hi = sb("qkT_hi", [P, KC + 1, S], F32R)
        qkT_lo = sb("qkT_lo", [P, KC + 1, S], F32R)
        q_stack = sb("q_stack", [98, H, S], F32R)
        k_stack = sb("k_stack", [98, KV, S], F32R)
        smax = sb("smax", [P, H, ST])
        m_hi = sb("m_hi", [H, S], F32R)
        m_lo = sb("m_lo", [H, S], F32R)
        probs = sb("probs", [P, 2, 2, ST, S])
        arden = sb("arden", [P, ST, HALF])
        x1 = sb("x1", [P, ST, D])
        stats1 = sb("stats1", [P, ST, 6])
        mv1 = sb("mv1", [P, ST, 2])
        rstd1 = sb("rstd1", [P, ST])
        x1T_hi, x1T_lo = qkT_hi[:, 0:KC, :], qkT_lo[:, 0:KC, :]

        ctxT_sb = sb("ctxT_sb", [P, KC, S])
        ctxT_hi = sb("ctxT_hi", [P, KC, S], F32R)
        ctxT_lo = sb("ctxT_lo", [P, KC, S], F32R)
        ctx_sb = sb("ctx_sb", [P, ST, H, VA])
        mq_stack = sb("mq_stack", [100, H, S], F32R)
        mk_stack = sb("mk_stack", [100, H, S], F32R)
        spare = probs[:, :, :, :, :].rearrange("p a b t s -> p (a b t) s")
        g_tmp = spare[0:H, 0:3, :]
        g_cumf, g_in, g_max, g_log = (spare[0:H, k, :] for k in range(3, 7))
        gates = spare[0:48, 7, :]
        g_hi = sb("g_hi", [H, S], F32R)
        g_lo = sb("g_lo", [H, S], F32R)
        gm_hi = sb("gm_hi", [H, S], F32R)
        gm_lo = sb("gm_lo", [H, S], F32R)
        floor = sb("floor", [P, ST, H])
        decay = sb("decay", [P, 2, 384])
        weighted = sb("weighted", [P, 3, 384])
        mrden = sb("mrden", [P, ST, HALF])
        hid = sb("hid", [P, ST, H, HD])
        sq = sb("sq", [P, ST, H, HD])
        att = hid[:, :, :, :].rearrange("p t h d -> p t (h d)")
        base = sq[:, :, :, :].rearrange("p t h d -> p t (h d)")
        hmean = sb("hmean", [P, ST * H])
        hvar = sb("hvar", [P, ST * H])
        stats2 = sb("stats2", [P, ST, 6])
        mv2 = sb("mv2", [P, ST, 2])
        rstd2 = sb("rstd2", [P, ST])
        x2 = sb("x2", [P, ST, D])
        x2T = sb("x2T", [P, KC, S])
        attT = x2T
        biased = sb("biased", [P, ST, E])
        top8 = sb("top8", [P, ST, 8])
        top8i = sb("top8i", [P, ST, 8], U32)
        tanh_sb = sb("tanh_sb", [P, S])
        silu_sb = sb("silu_sb", [P, S])
        hT = sb("hT", [P, SC, S])
        gw_f = hT[:, :, :].rearrange("p c (a n) -> p (c a) n", n=P)

        ps = ctx.enter_context(nc.psum_tensor("ps", [P, 8, 512], F32))

        w_in = sig("w_in", 16 * 16)
        fill_out = sig("fill_out", 16)
        consts = sig("consts", 1)
        fills = sig("fills", 1)
        gsum = sig("gsum", 1)
        gwhi = sig("gwhi", 1)
        gwlo = sig("gwlo", 1)
        pro = sig("pro", 1)
        xT_in, x_in, ctxT_in, ctx_row_in = sig("xT_in", 16), sig("x_in", 16), sig("ctxT_in", 16), sig("ctx_row_in", 32)
        qkv_ready = sig("qkv_ready", ST)
        pass_done = sig("pass_done", ST)
        rope_step = sig("rope_step", ST)
        rope_done = sig("rope_done", ST)
        qkT_ready = sig("qkT_ready", 2)
        qk_hi_done, qk_lo_done = sig("qk_hi_done", 2), sig("qk_lo_done", 2)
        q_in, k_in = sig("q_in", 12 * 16), sig("k_in", 12 * 16)
        s_ready, smax_done = sig("s_ready", PAIRS), sig("smax_done", PAIRS)
        m_ready, m_hi_done, m_lo_done, m_in = sig("m_ready", 1), sig("m_hi_done", 1), sig("m_lo_done", 1), sig("m_in", 32)
        t_ready, p_done = sig("t_ready", PAIRS), sig("p_done", PAIRS)
        av_pair = sig("av_pair", PAIRS)
        arden_done, att_done = sig("arden_done", 2), sig("att_done", 2)
        attT_ready, attT_done = sig("attT_ready", 1), sig("attT_done", 1)
        wo_ready, h_done = sig("wo_ready", ST), sig("h_done", ST)
        ln1_step, mv1_done, rstd1_step, rstd1_done = sig("ln1_step", ST), sig("mv1_done", ST), sig("rstd1_step", 1), sig("rstd1_done", 1)
        x1_done = sig("x1_done", ST)
        x1T_ready, x1T_hi_done, x1T_lo_done = sig("x1T_ready", 1), sig("x1T_hi_done", 1), sig("x1T_lo_done", 1)
        ctx_hi_done, ctx_lo_done = sig("ctx_hi_done", 1), sig("ctx_lo_done", 1)
        mk_in = sig("mk_in", 12 * 16)
        mq_in = sig("mq_in", 12 * 16)
        gates_ready, gates_done = sig("gates_ready", 1), sig("gates_done", 1)
        gabs_done, gexp_done, gln_done = sig("gabs_done", 1), sig("gexp_done", 1), sig("gln_done", 1)
        g_step, g_rows, row_in = sig("g_step", 6), sig("g_rows", 1), sig("row_in", 64)
        glog_ready, floor_done = sig("glog_ready", 1), sig("floor_done", 1)
        qk2_ready, decay_ready = sig("qk2_ready", H), sig("decay_ready", H)
        decay_done, weighted_done = sig("decay_done", H), sig("weighted_done", H)
        av2_head = sig("av2_head", H)
        mrden_step, mh_done = sig("mrden_step", 8), sig("mh_done", 2)
        hmean_step, hmean_done = sig("hmean_step", 1), sig("hmean_done", 1)
        hsub_done, hsq_done = sig("hsub_done", 1), sig("hsq_done", 1)
        hvar_step, hvar_done = sig("hvar_step", 1), sig("hvar_done", 1)
        y_step, y_done = sig("y_step", 3), sig("y_done", 1)
        ln2_step, mv2_done, rstd2_step, rstd2_done = sig("ln2_step", ST), sig("mv2_done", ST), sig("rstd2_step", 1), sig("rstd2_done", 1)
        x2_done, x2_out = sig("x2_done", ST), sig("x2_out", 16)
        x2T_ready, x2T_done = sig("x2T_ready", 1), sig("x2T_done", 1)
        lg_ready, lg_done = sig("lg_ready", 1), sig("lg_done", 1)
        top_step, choice_done = sig("top_step", 5), sig("choice_done", 1)
        ug_ready, tanh_done, silu_done, hT_done = sig("ug_ready", SC), sig("tanh_done", SC), sig("silu_done", SC), sig("hT_done", SC)
        sd_ready, base_done, base_out = sig("sd_ready", ST), sig("base_done", ST), sig("base_out", 16)

        x_v = x.rearrange("(b t p) d -> b p t d", t=ST, p=P)
        ctx_v = ctx_in.rearrange("(b t p) (h d) -> b t p h d", t=ST, p=P, d=HD)
        x2_v = x2_dram.rearrange("(b t p) d -> b p t d", t=ST, p=P)
        base_v = base_dram.rearrange("(b t p) d -> b p t d", t=ST, p=P)

        def one(v, b):
            return v[b] if isinstance(b, int) else v[bass.ds(b, 1)].rearrange(
                {4: "o p t d -> (o p) t d", 5: "o t p h d -> (o t) p h d"}[len(v.shape)])

        def run(eng, body):
            body(0, None, True)
            body(1, 0, True)
            with eng.Fori(2, B - 1) as i:
                body(i, i - 1, True)
            body(B - 1, B - 2, False)
            body(None, B - 1, False)

        block = ctx.enter_context(nc.Block())

        @block.sync
        def _(sp):
            loads = [(wqkv_sb[:, :, :], wqkv), (wo_sb[:, :, :], wo), (su_sb[:, :, :], su), (sg_sb[:, :, :], sg),
                     (sd_sb[:, :, :], sd), (rw_sb[:, :, :], router_w), (rb_sb[:, :], router_b.partition_broadcast(P)),
                     (lns_sb[:, :], ln_scale.partition_broadcast(P)), (cos_sb[:, :, :], rope_cos),
                     (sin_sb[:, :, :, :], rope_sin), (id_sb[:, :], ident), (mask_sb[:, :], mask),
                     (gw_raw[:, :, :, :], gate_w), (gb_sb[0:H, :], gate_b[0]), (gb_sb[32:48, :], gate_b[1])]
            sp.wait_ge(consts.sem, 1)
            for dst, src in loads:
                sp.dma_start(dst, src).then_inc(w_in.sem, 16)
            sp.dma_start(xT_sb[:, :, :], xT[0]).then_inc(xT_in.sem, 16)

            def stack(dst, hi, lo, chunk, done, order):
                for row, part in enumerate(order):
                    src = hi if part == "hi" else lo
                    for j in range(GQ):
                        if chunk is None:
                            d, s = dst[32 * row:32 * row + 32, j::GQ, :], src[32 * j:32 * j + 32, 0:KC, :]
                        else:
                            d, s = dst[32 * row:32 * row + 32, j, :], src[32 * j:32 * j + 32, chunk, :]
                        sp.dma_start(d.bitcast(F32), s.bitcast(F32)).then_inc(done.sem, 16)

            Q_ROWS, K_ROWS = ("hi", "hi", "lo"), ("hi", "lo", "hi")

            def body(b, y, more):
                if y is not None:
                    wait(sp, x1T_hi_done, y, 1)
                    wait(sp, x1T_lo_done, y, 1)
                    wait(sp, decay_ready, y, 0)
                    stack(mq_stack, x1T_hi, x1T_lo, None, mq_in, Q_ROWS)
                if b is not None and more:
                    wait(sp, qkv_ready, b, ST)
                    sp.dma_start(xT_sb[:, :, :], one(xT, b + 1)).then_inc(xT_in.sem, 16)
                if y is not None:
                    wait(sp, g_rows, y, 1)
                    wait(sp, mq_in, y, 12 * 16)
                    for row, src in ((96, g_hi), (97, g_lo)):
                        sp.dma_start(mk_stack[row:row + 1, :, :].bitcast(F32), src[:, :].bitcast(F32))\
                            .then_inc(row_in.sem, 16)
                    for row, src in ((98, gm_hi), (99, gm_lo)):
                        sp.dma_start(mq_stack[row:row + 1, :, :].bitcast(F32), src[:, :].bitcast(F32))\
                            .then_inc(row_in.sem, 16)
                if b is not None:
                    wait(sp, t_ready, b, 0)
                    wait(sp, qk_hi_done, b, 2)
                    wait(sp, qk_lo_done, b, 2)
                    stack(q_stack, qkT_hi, qkT_lo, None, q_in, Q_ROWS)
                    stack(k_stack, qkT_hi, qkT_lo, KC, k_in, K_ROWS)
                    if y is not None:
                        wait(sp, decay_ready, y, H)
                    wait(sp, ctx_hi_done, b, 1)
                    wait(sp, ctx_lo_done, b, 1)
                    stack(mk_stack, ctxT_hi, ctxT_lo, None, mk_in, K_ROWS)
                    wait(sp, m_hi_done, b, 1)
                    wait(sp, m_lo_done, b, 1)
                    for row, src in ((96, m_hi), (97, m_lo)):
                        sp.dma_start(q_stack[row:row + 1, :, :].bitcast(F32), src[:, :].bitcast(F32))\
                            .then_inc(m_in.sem, 16)

            run(sp, body)

        @block.gpsimd
        def _(pool):
            rest = (pool.alloc_register("rest"), consts.sem)
            nc.gpsimd.memset(gb_sb[:, :], 0.0).then_inc(consts.sem, 1)
            nc.gpsimd.memset(gw_f[:, :, :], 0.0).then_inc(fills.sem, 1)
            nc.gpsimd.memset(ones_row[:, :], 1.0).then_inc(pro.sem, 1)
            nc.gpsimd.memset(eps_half[:, :], -0.5).then_inc(pro.sem, 1)
            nc.gpsimd.memset(v_sb[:, :, :, :], 1.0).then_inc(pro.sem, 1)
            nc.gpsimd.memset(ctx_sb[:, :, :, :], 1.0).then_inc(pro.sem, 1)
            nc.gpsimd.memset(sq[:, 0, :, :], 0.0).then_inc(fills.sem, 1)
            pool.wait_ge(fills.sem, 2)
            xs_v = xs_dram.rearrange("(t p) d -> p t d", p=P)
            zero_rows = sq[:, 0, :, :].rearrange("p h d -> p (h d)").unsqueeze(1).to_broadcast([P, FILL, D])
            for t in range(0, MT, FILL):
                pool.dma_start(xs_v[:, t:t + FILL, :], zero_rows).then_inc(fill_out.sem, 16)
            pool.dma_start(x_sb[:, :, :], x_v[0]).then_inc(x_in.sem, 16)
            pool.dma_start(ctxT_sb[:, :, :], ctxT[0]).then_inc(ctxT_in.sem, 16)
            pool.wait_ge(pro.sem, 4)
            pool.wait_ge(w_in.sem, 15 * 16)
            for g in range(2):
                nc.gpsimd.tensor_copy(gw_f[:, 0:KC, 32 * g:32 * g + H], gw_raw[:, 0:KC, g, :]).then_inc(gsum.sem, 1)
                nc.gpsimd.tensor_tensor(gw_f[:, KC:2 * KC, 32 * g:32 * g + H], gw_raw[:, KC:2 * KC, g, :],
                                        gw_raw[:, 2 * KC:3 * KC, g, :], ALU.add).then_inc(gsum.sem, 1)

            def body(b, y, more):
                if b is not None:
                    wait(pool, ctxT_in, b, 16)
                    if y is not None:
                        wait(pool, gates_ready, y, 1)
                        wait(pool, mk_in, y, 12 * 16, rest=rest)
                    nc.gpsimd.tensor_copy(ctxT_hi[:, :, :], ctxT_sb[:, :, :]).then_inc(ctx_hi_done.sem, 1)
                    wait(pool, ctx_hi_done, b, 1)
                    nc.gpsimd.tensor_tensor(ctxT_lo[:, :, :], ctxT_sb[:, :, :], ctxT_hi[:, :, :].bitcast(F32),
                                            ALU.subtract).then_inc(ctx_lo_done.sem, 1)
                    if more:
                        wait(pool, ctx_lo_done, b, 1, rest=rest)
                        pool.dma_start(ctxT_sb[:, :, :], one(ctxT, b + 1)).then_inc(ctxT_in.sem, 16)
                    if y is not None:
                        wait(pool, av2_head, y, H, rest=rest)
                    for t in range(ST):
                        pool.dma_start(ctx_sb[:, t, :, 0:HD], ctx_v[b, t] if isinstance(b, int) else
                                       ctx_v[bass.ds(b, 1), t].rearrange("o p h d -> (o p) h d"))\
                            .then_inc(ctx_row_in.sem, 16)
                if y is not None:
                    hv = hid[:, :, :, :].rearrange("p t h d -> p (t h) d")
                    sv = sq[:, :, :, :].rearrange("p t h d -> p (t h) d")
                    wide = [P, ST * H, HD]
                    wait(pool, hmean_done, y, 1)
                    nc.gpsimd.tensor_tensor(hv, hv, bcast(hmean[:, :], wide), ALU.subtract).then_inc(hsub_done.sem, 1)
                    wait(pool, hsub_done, y, 1)
                    wait(pool, base_out, y, 0)
                    nc.gpsimd.tensor_tensor(sv, hv, hv, ALU.mult).then_inc(hsq_done.sem, 1)
                    wait(pool, hvar_done, y, 1)
                    step = Steps(pool, y_step, y)
                    step(nc.gpsimd.tensor_tensor(hvar[:, :], hvar[:, :], eps_half[:, :], ALU.pow))
                    step(nc.gpsimd.tensor_tensor(hv, hv, bcast(hvar[:, :], wide), ALU.mult))
                    hf = hid[:, :, :, :].rearrange("p t h d -> p t (h d)")
                    step(nc.gpsimd.tensor_tensor(hf, hf, lns_sb[:, :].unsqueeze(1).to_broadcast([P, ST, D]), ALU.mult))
                    step.end()
                    wait(pool, x2_out, y, 0)
                    wait(pool, base_done, y, 0)
                    nc.gpsimd.tensor_tensor(x2[:, :, :], hf, x1[:, :, :], ALU.add).then_inc(y_done.sem, 1)
                    wait(pool, mv2_done, y, ST, rest=rest)
                    step = Steps(pool, rstd2_step, y)
                    step(nc.gpsimd.tensor_scalar(rstd2[:, :], mv2[:, :, 1], LN_EPS, None, ALU.add))
                    step.end()
                    nc.gpsimd.tensor_tensor(rstd2[:, :], rstd2[:, :], eps_half[:, 0:ST], ALU.pow).then_inc(rstd2_done.sem, 1)
                    wait(pool, x2_done, y, ST, rest=rest)
                    pool.dma_start(one(x2_v, y), x2[:, :, :]).then_inc(x2_out.sem, 16)
                if b is not None:
                    wait(pool, mv1_done, b, ST, rest=rest)
                    step = Steps(pool, rstd1_step, b)
                    step(nc.gpsimd.tensor_scalar(rstd1[:, :], mv1[:, :, 1], LN_EPS, None, ALU.add))
                    step.end()
                    nc.gpsimd.tensor_tensor(rstd1[:, :], rstd1[:, :], eps_half[:, 0:ST], ALU.pow).then_inc(rstd1_done.sem, 1)
                    if more:
                        pool.dma_start(x_sb[:, :, :], one(x_v, b + 1)).then_inc(x_in.sem, 16)
                if y is not None:
                    wait(pool, base_done, y, ST, rest=rest)
                    pool.dma_start(one(base_v, y), base[:, :, :]).then_inc(base_out.sem, 16)

            body(0, None, True)
            pool.wait_ge(fill_out.sem, 16 * (MT // FILL))
            body(1, 0, True)
            with pool.Fori(2, B - 1) as i:
                body(i, i - 1, True)
            body(B - 1, B - 2, False)
            body(None, B - 1, False)
            pool.wait_ge(x2_out.sem, 16 * B)
            pool.wait_ge(base_out.sem, 16 * B)

        @block.scalar
        def _(act):
            act.wait_ge(w_in.sem, 15 * 16)
            nc.scalar.copy(idr_sb[:, :], id_sb[:, :]).then_inc(consts.sem, 1)
            nc.scalar.copy(maskr_sb[:, :], mask_sb[:, :]).then_inc(consts.sem, 1)
            act.wait_ge(gsum.sem, 4)
            nc.scalar.copy(gw_hi[:, :, :], gw_f[:, :, :]).then_inc(gwhi.sem, 1)
            act.wait_ge(pro.sem, 4)

            def body(b, y, more):
                def pass_through(t):
                    wait(act, qkv_ready, b, t + 1)
                    if t == 0:
                        wait(act, qkT_ready, b, 0)
                        wait(act, av_pair, b, 0)
                    qkv = ps[:, 2 * t:2 * t + 2, :].rearrange("p a n -> p (a n)")
                    nc.scalar.copy(qk_sb[:, t, :, ROT:], qkv[:, 0:QKH * HD].rearrange("p (h d) -> p h d", d=HD)[:, :, ROT:])
                    nc.scalar.copy(v_sb[:, t, :, 0:HD], qkv[:, QKH * HD:QKV].rearrange("p (h d) -> p h d", d=HD))\
                        .then_inc(pass_done.sem, 1)

                if b is not None:
                    pass_through(0)
                if y is not None:
                    wait(act, gabs_done, y, 1)
                    nc.scalar.activation(g_tmp[:, 1, :], g_tmp[:, 0, :], ACT.Exp).then_inc(gexp_done.sem, 1)
                    wait(act, gexp_done, y, 1)
                    nc.scalar.activation(g_tmp[:, 2, :], g_tmp[:, 1, :], ACT.Ln, bias=1.0).then_inc(gln_done.sem, 1)
                if b is not None:
                    pass_through(1)
                if b is not None:
                    wait(act, q_in, b, 0)
                    wait(act, k_in, b, 0)
                    if y is not None:
                        wait(act, mq_in, y, 12 * 16)
                    wait(act, qkT_ready, b, 1)
                    nc.scalar.copy(qkT_hi[:, 0:KC, :], ps[:, 6:8, :].rearrange("p a (c s) -> p (a c) s", s=S))\
                        .then_inc(qk_hi_done.sem, 1)
                    wait(act, qkT_ready, b, 2)
                    nc.scalar.copy(qkT_hi[:, KC, :], ps[:, 5, 0:S]).then_inc(qk_hi_done.sem, 1)
                if y is not None:
                    wait(act, glog_ready, y, 1)
                    nc.scalar.activation(floor[:, :, :], ps[:, 4, S:S + ST * H].rearrange("p (t h) -> p t h", h=H),
                                         ACT.Exp, scale=-1.0).then_inc(floor_done.sem, 1)
                    for h in range(H):
                        wait(act, decay_ready, y, h + 1)
                        if h >= 2:
                            wait(act, weighted_done, y, h - 1)
                        else:
                            wait(act, weighted_done, y, 0)
                        nc.scalar.activation(decay[:, h % 2, :], ps[:, 2 + h % 2, 0:384], ACT.Exp).then_inc(decay_done.sem, 1)

                def exp_pair(i):
                    wait(act, t_ready, b, i + 1)
                    if i >= 2:
                        wait(act, av_pair, b, i - 1)
                    for j in range(2):
                        ins = nc.scalar.activation(probs[:, i % 2, j, :, :],
                                                   ps[:, 2 * (i % 2) + j, :].rearrange("p (t s) -> p t s", s=S),
                                                   ACT.Exp, scale=SCALE)
                    ins.then_inc(p_done.sem, 1)

                def tanh(c):
                    wait(act, ug_ready, y, c + 1)
                    wait(act, silu_done, y, c)
                    nc.scalar.activation(tanh_sb[:, :], ps[:, 6 + c % 2, 0:S], ACT.Tanh, scale=0.5).then_inc(tanh_done.sem, 1)

                if b is not None:
                    exp_pair(0)
                    exp_pair(1)
                if y is not None:
                    wait(act, x2T_ready, y, 1)
                    wait(act, ug_ready, y, 0)
                    nc.scalar.copy(x2T[:, :, :], ps[:, 4:6, :].rearrange("p a (c s) -> p (a c) s", s=S)).then_inc(x2T_done.sem, 1)
                for c in range(SC):
                    if b is not None and 2 * c + 2 < PAIRS:
                        exp_pair(2 * c + 2)
                    if y is not None:
                        tanh(c)
                    if b is not None and 2 * c + 3 < PAIRS:
                        exp_pair(2 * c + 3)
                if b is not None:
                    wait(act, attT_ready, b, 1)
                    wait(act, wo_ready, b, 0)
                    nc.scalar.copy(attT[:, :, :], ps[:, 4:6, :].rearrange("p a (c s) -> p (a c) s", s=S)).then_inc(attT_done.sem, 1)
                    wait(act, x1T_ready, b, 1)
                    if y is not None:
                        wait(act, gates_ready, y, 1)
                        wait(act, mq_in, y, 12 * 16)
                    nc.scalar.copy(x1T_hi[:, :, :], ps[:, 4:6, :].rearrange("p a (c s) -> p (a c) s", s=S))\
                        .then_inc(x1T_hi_done.sem, 1)

            run(act, body)

        @block.vector
        def _(dve):
            rest = (dve.alloc_register("rest"), gwhi.sem)
            dve.wait_ge(gwhi.sem, 1)
            nc.vector.tensor_tensor(gw_lo[:, :, :], gw_f[:, :, :], gw_hi[:, :, :].bitcast(F32), ALU.subtract).then_inc(gwlo.sem, 1)
            nc.vector.memset(k_stack[96:98, :, :].bitcast(F32), -1.0).then_inc(gwlo.sem, 1)
            nc.vector.memset(mk_stack[96:100, :, :].bitcast(F32), -1.0).then_inc(gwlo.sem, 1)
            nc.vector.memset(mq_stack[96:100, :, :].bitcast(F32), 1.0).then_inc(gwlo.sem, 1)
            dve.wait_ge(pro.sem, 4)

            def body(b, y, more):
                def rope(t):
                    wait(dve, pass_done, b, t + 1)
                    if t == 0:
                        wait(dve, qkT_ready, b, 0)
                    else:
                        wait(dve, rope_done, b, t)
                    qk = ps[:, 2 * t:2 * t + 2, :].rearrange("p a n -> p (a n)")[:, 0:QKH * HD].rearrange("p (h d) -> p h d", d=HD)
                    pr = qk[:, :, 0:ROT].rearrange("p h (i two) -> p h i two", two=2)
                    nc.vector.tensor_tensor(rope_a[:, :, :], qk[:, :, 0:ROT],
                                            cos_sb[:, t, :].unsqueeze(1).to_broadcast([P, QKH, ROT]), ALU.mult)
                    half = [P, QKH, ROT // 2]
                    nc.vector.tensor_tensor(rope_b[:, :, :, 0], pr[:, :, :, 1],
                                            sin_sb[:, t, 0, :].unsqueeze(1).to_broadcast(half), ALU.mult)
                    nc.vector.tensor_tensor(rope_b[:, :, :, 1], pr[:, :, :, 0],
                                            sin_sb[:, t, 1, :].unsqueeze(1).to_broadcast(half), ALU.mult).then_inc(rope_step.sem, 1)
                    wait(dve, rope_step, b, t + 1)
                    nc.vector.tensor_tensor(qk_sb[:, t, :, 0:ROT], rope_a[:, :, :],
                                            rope_b[:, :, :, :].rearrange("p h i two -> p h (i two)"), ALU.add)\
                        .then_inc(rope_done.sem, 1)

                if b is not None:
                    rope(0)
                if y is not None:
                    wait(dve, gates_ready, y, 1)
                    nc.vector.tensor_scalar(gates, ps[0:48, 4, 0:S], gb_sb[:, :], None, ALU.add).then_inc(gates_done.sem, 1)
                    wait(dve, gates_done, y, 1)
                    nc.vector.scalar_tensor_tensor(g_tmp[:, 0, :], gates[32:48, :], -1.0, gates[32:48, :], ALU.mult, ALU.min).then_inc(gabs_done.sem, 1)
                if b is not None:
                    rope(1)
                if y is not None:
                    step = Steps(dve, g_step, y)
                    step(nc.vector.tensor_scalar(g_cumf, gates[32:48, :], 0.0, None, ALU.min))
                    wait(dve, gln_done, y, 1)
                    wait(dve, row_in, y, 0)
                    step(nc.vector.tensor_tensor(g_in, g_cumf, g_tmp[:, 2, :], ALU.subtract))
                    step(nc.vector.tensor_tensor_scan(g_cumf, ones_row[:, :], g_in, 0.0, ALU.mult, ALU.add))
                    step(nc.vector.tensor_tensor(g_in, gates[0:H, :], g_cumf, ALU.subtract))
                    step(nc.vector.tensor_tensor_scan(g_max, g_in, g_in, -3.0e38, ALU.max, ALU.max))
                    nc.vector.tensor_tensor(g_log, g_cumf, g_max, ALU.add)
                    nc.vector.tensor_copy(g_hi[:, :], g_in)
                    step(nc.vector.tensor_copy(gm_hi[:, :], g_max))
                    nc.vector.tensor_tensor(g_lo[:, :], g_in, g_hi[:, :].bitcast(F32), ALU.subtract)
                    nc.vector.tensor_tensor(gm_lo[:, :], g_max, gm_hi[:, :].bitcast(F32), ALU.subtract).then_inc(g_rows.sem, 1)
                    step.end()
                if b is not None:
                    wait(dve, q_in, b, 0)
                    wait(dve, k_in, b, 0)
                    wait(dve, qk_hi_done, b, 1)
                    nc.vector.tensor_tensor(qkT_lo[:, 0:KC, :], ps[:, 6:8, :].rearrange("p a (c s) -> p (a c) s", s=S),
                                            qkT_hi[:, 0:KC, :].bitcast(F32), ALU.subtract).then_inc(qk_lo_done.sem, 1)
                    wait(dve, qk_hi_done, b, 2)
                    nc.vector.tensor_tensor(qkT_lo[:, KC, :], ps[:, 5, 0:S], qkT_hi[:, KC, :].bitcast(F32),
                                            ALU.subtract).then_inc(qk_lo_done.sem, 1)

                def normalise(half, step):
                    wait(dve, av2_head, y, HALF * (half + 1))
                    if half == 0:
                        wait(dve, floor_done, y, 1)
                        wait(dve, y_done, y, 0)
                    o = ps[:, 4 + 2 * half:6 + 2 * half, 0:HALF * VA].rearrange("p t (h c) -> p t h c", c=VA)
                    hs = slice(HALF * half, HALF * (half + 1))
                    step(nc.vector.scalar_tensor_tensor(mrden[:, :, :], o[:, :, :, HD], -1.0, floor[:, :, hs], ALU.mult, ALU.max))
                    step(nc.vector.tensor_tensor(mrden[:, :, :], o[:, :, :, HD], mrden[:, :, :], ALU.max))
                    step(nc.vector.tensor_scalar(mrden[:, :, :], mrden[:, :, :], ML_EPS, None, ALU.add))
                    step(nc.vector.reciprocal(mrden[:, :, :], mrden[:, :, :]))
                    for t in range(ST):
                        ins = nc.vector.tensor_tensor(hid[:, t, hs, :], o[:, t, :, 0:HD], bcast(mrden[:, t, :], [P, HALF, HD]), ALU.mult)
                    ins.then_inc(mh_done.sem, 1)

                if y is not None:
                    step = Steps(dve, mrden_step, y)
                    for h in range(H):
                        wait(dve, decay_done, y, h + 1)
                        wait(dve, qk2_ready, y, h + 1)
                        if h >= 3:
                            wait(dve, av2_head, y, h - 2)
                        nc.vector.scalar_tensor_tensor(weighted[:, h % 3, :], ps[:, h % 2, 0:384], SCALE,
                                                       decay[:, h % 2, :], ALU.mult, ALU.mult).then_inc(weighted_done.sem, 1)
                        if h == HALF + 3:
                            normalise(0, step)
                    normalise(1, step)
                    step.end()

                def max_pair(i):
                    wait(dve, s_ready, b, i + 1)
                    nc.vector.tensor_reduce(smax[:, 2 * i:2 * i + 2, :],
                                            ps[:, 2 * (i % 2):2 * (i % 2) + 2, :].rearrange("p a (t s) -> p a t s", s=S),
                                            AX.X, ALU.max).then_inc(smax_done.sem, 1)

                if b is not None:
                    wait(dve, m_ready, b, 0)
                    max_pair(0)
                hv = hid[:, :, :, :].rearrange("p t h d -> p (t h) d")
                sv = sq[:, :, :, :].rearrange("p t h d -> p (t h) d")
                if y is not None:
                    wait(dve, mh_done, y, 2)
                    nc.vector.tensor_reduce(hmean[:, :], hv, AX.X, ALU.add).then_inc(hmean_step.sem, 1)
                    wait(dve, hmean_step, y, 1)
                    nc.vector.tensor_scalar(hmean[:, :], hmean[:, :], 1.0 / HD, None, ALU.mult).then_inc(hmean_done.sem, 1)
                if b is not None:
                    for i in range(1, 4):
                        max_pair(i)
                if y is not None:
                    wait(dve, hsq_done, y, 1)
                    nc.vector.tensor_reduce(hvar[:, :], sv, AX.X, ALU.add).then_inc(hvar_step.sem, 1)
                    wait(dve, hvar_step, y, 1)
                    nc.vector.tensor_scalar(hvar[:, :], hvar[:, :], 1.0 / HD, ML_EPS, ALU.mult, ALU.add).then_inc(hvar_done.sem, 1)
                if b is not None:
                    for i in range(4, PAIRS):
                        max_pair(i)
                    wait(dve, m_ready, b, 1)
                    wait(dve, m_in, b, 0)
                    nc.vector.tensor_copy(m_hi[:, :], ps[0:H, 6, 0:S]).then_inc(m_hi_done.sem, 1)
                    wait(dve, m_hi_done, b, 1)
                    nc.vector.tensor_tensor(m_lo[:, :], ps[0:H, 6, 0:S], m_hi[:, :].bitcast(F32), ALU.subtract).then_inc(m_lo_done.sem, 1)

                if y is not None:
                    wait(dve, y_done, y, 1)
                    for t in range(ST):
                        nc.vector.bn_stats(stats2[:, t, :], x2[:, t, :]).then_inc(ln2_step.sem, 1)
                    for t in range(ST):
                        wait(dve, ln2_step, y, t + 1, rest=rest)
                        nc.vector.bn_aggr(mv2[:, t, :], stats2[:, t, :]).then_inc(mv2_done.sem, 1)
                    wait(dve, rstd2_done, y, 1)
                    for t in range(ST):
                        nc.vector.tensor_scalar(x2[:, t, :], x2[:, t, :], mv2[:, t, 0:1], rstd2[:, t:t + 1],
                                                ALU.subtract, ALU.mult).then_inc(x2_done.sem, 1)
                    wait(dve, lg_ready, y, 1)
                    lg = ps[:, 7, 0:ST * E].rearrange("p (t e) -> p t e", e=E)
                    step = Steps(dve, top_step, y)
                    nc.vector.tensor_copy(logits[:, bass.ds(y * ST, ST), :], lg)
                    nc.vector.tensor_tensor(biased[:, :, :], lg, rb_sb[:, :].unsqueeze(1).to_broadcast([P, ST, E]), ALU.add)\
                        .then_inc(lg_done.sem, 1)
                    wait(dve, lg_done, y, 1, rest=rest)
                    for t in range(ST):
                        step(nc.vector.max(top8[:, t, :], biased[:, t, :]), rest=rest)
                        step(nc.vector.max_index(top8i[:, t, :], top8[:, t, :], biased[:, t, :]), rest=rest)
                    step(nc.vector.tensor_copy(choice[:, bass.ds(y * ST, ST), :], top8i[:, :, 0:TOPK]))
                    step.end()

                def average(half):
                    wait(dve, av_pair, b, PAIRS // 2 * (half + 1))
                    if half == 0:
                        wait(dve, attT_ready, b, 0)
                    o = ps[:, 4:6, 0:HALF * VA].rearrange("p t (h c) -> p t h c", c=VA)
                    nc.vector.reciprocal(arden[:, :, :], o[:, :, :, HD]).then_inc(arden_done.sem, 1)
                    wait(dve, arden_done, b, half + 1)
                    for t in range(ST):
                        ins = nc.vector.tensor_tensor(
                            att[:, t, D // 2 * half:D // 2 * (half + 1)].rearrange("p (h d) -> p h d", d=HD),
                            o[:, t, :, 0:HD], bcast(arden[:, t, :], [P, HALF, HD]), ALU.mult)
                    ins.then_inc(att_done.sem, 1)

                for c in range(SC):
                    if b is not None and c == 2:
                        average(0)
                    if y is not None:
                        wait(dve, tanh_done, y, c + 1)
                        wait(dve, hT_done, y, c)
                        nc.vector.scalar_tensor_tensor(silu_sb[:, :], tanh_sb[:, :], 1.0, ps[:, 6 + c % 2, 0:S],
                                                       ALU.add, ALU.mult).then_inc(silu_done.sem, 1)
                        wait(dve, silu_done, y, c + 1)
                        if c == 0:
                            wait(dve, sd_ready, y, 0)
                        nc.vector.scalar_tensor_tensor(hT[:, c, :], silu_sb[:, :], 0.5, ps[:, 6 + c % 2, S:2 * S],
                                                       ALU.mult, ALU.mult).then_inc(hT_done.sem, 1)
                if b is not None:
                    average(1)

                def add_base(t):
                    wait(dve, sd_ready, y, t + 1)
                    if t == 0:
                        wait(dve, base_out, y, 0)
                    nc.vector.tensor_tensor(base[:, t, :], ps[:, 2 + t, :], x2[:, t, :], ALU.add).then_inc(base_done.sem, 1)

                if y is not None:
                    add_base(0)
                if b is not None:
                    wait(dve, x_in, b, 16)
                    for t in range(ST):
                        wait(dve, wo_ready, b, t + 1)
                        nc.vector.tensor_tensor(x1[:, t, :], ps[:, t, :], x_sb[:, t, :], ALU.add).then_inc(h_done.sem, 1)
                    for t in range(ST):
                        wait(dve, h_done, b, t + 1)
                        nc.vector.bn_stats(stats1[:, t, :], x1[:, t, :]).then_inc(ln1_step.sem, 1)
                    for t in range(ST):
                        wait(dve, ln1_step, b, t + 1, rest=rest)
                        nc.vector.bn_aggr(mv1[:, t, :], stats1[:, t, :]).then_inc(mv1_done.sem, 1)
                if y is not None:
                    add_base(1)
                if b is not None:
                    wait(dve, rstd1_done, b, 1)
                    for t in range(ST):
                        nc.vector.tensor_scalar(x1[:, t, :], x1[:, t, :], mv1[:, t, 0:1], rstd1[:, t:t + 1],
                                                ALU.subtract, ALU.mult).then_inc(x1_done.sem, 1)
                    wait(dve, x1T_hi_done, b, 1)
                    nc.vector.tensor_tensor(x1T_lo[:, :, :], ps[:, 4:6, :].rearrange("p a (c s) -> p (a c) s", s=S),
                                            x1T_hi[:, :, :].bitcast(F32), ALU.subtract).then_inc(x1T_lo_done.sem, 1)

            run(dve, body)

        @block.tensor
        def _(pe):
            rest = (pe.alloc_register("rest"), consts.sem)
            pe.wait_ge(w_in.sem, 15 * 16)
            pe.wait_ge(consts.sem, 3)
            pe.wait_ge(gwlo.sem, 4)

            def body(b, y, more):
                def qkv(t):
                    for lo, hi in ((0, 512), (512, QKV)):
                        for c in range(KC):
                            ins = nc.tensor.matmul(ps[:, 2 * t + lo // 512, 0:hi - lo], xT_sb[:, c, P * t:P * t + P],
                                                   wqkv_sb[:, c, lo:hi], start=c == 0, stop=c == KC - 1)
                    ins.then_inc(qkv_ready.sem, 1)

                if b is not None:
                    wait(pe, xT_in, b, 16)
                    wait(pe, h_done, b, 0)
                    qkv(0)
                if y is not None:
                    wait(pe, x1T_hi_done, y, 1)
                    wait(pe, x1T_lo_done, y, 1)
                    wait(pe, ctx_lo_done, y, 1)
                    n = 0
                    for side, (hi, lo) in enumerate(((x1T_hi, x1T_lo), (ctxT_hi, ctxT_lo))):
                        for c in range(KC):
                            for w, v in ((gw_hi, hi), (gw_lo, hi), (gw_hi, lo)):
                                ins = nc.tensor.matmul(ps[:, 4, 0:S], w[:, KC * side + c, :], v[:, c, :],
                                                       start=n == 0, stop=n == 6 * KC - 1)
                                n += 1
                    ins.then_inc(gates_ready.sem, 1)
                if b is not None:
                    if y is not None:
                        wait(pe, base_done, y, 0)
                    qkv(1)
                    for t in range(ST):
                        wait(pe, rope_done, b, t + 1)
                        wait(pe, pass_done, b, t + 1)
                    if y is not None:
                        wait(pe, hT_done, y, 0)
                    for c in range(KC):
                        for t in range(ST):
                            ins = nc.tensor.transpose(ps[:, 6 + c // 2, S * (c % 2) + P * t:S * (c % 2) + P * t + P],
                                                      qk_sb[:, t, GQ * c:GQ * c + GQ, :].rearrange("p h d -> p (h d)"), id_sb[:, :])
                    ins.then_inc(qkT_ready.sem, 1)
                    for t in range(ST):
                        ins = nc.tensor.transpose(ps[:, 5, P * t:P * t + P],
                                                  qk_sb[:, t, H:QKH, :].rearrange("p h d -> p (h d)"), id_sb[:, :])
                    ins.then_inc(qkT_ready.sem, 1)

                def decay_mm(h):
                    if h == 0:
                        wait(pe, row_in, y, 64)
                    if h >= 2:
                        wait(pe, decay_done, y, h - 1)
                    bank = ps[:, 2 + h % 2, :]
                    for t, cols in ((0, slice(0, S)), (1, slice(S, 384))):
                        nc.tensor.matmul(bank[:, cols], mk_stack[96:100, h, P * t:P * t + P], mq_stack[96:100, h, P * t:S],
                                         start=True, stop=False)
                        ins = nc.tensor.matmul(bank[:, cols.start:cols.start + P], idr_sb[:, :], maskr_sb[:, :],
                                               start=False, stop=True)
                    ins.then_inc(decay_ready.sem, 1)

                def qk2_mm(h):
                    if h == 0:
                        wait(pe, mq_in, y, 12 * 16)
                        wait(pe, mk_in, y, 12 * 16)
                        if b is not None:
                            wait(pe, rope_done, b, ST)
                    if h >= 2:
                        wait(pe, weighted_done, y, h - 1)
                    for t, cols in ((0, slice(0, S)), (1, slice(S, 384))):
                        ins = nc.tensor.matmul(ps[:, h % 2, cols], mk_stack[0:96, h, P * t:P * t + P], mq_stack[0:96, h, P * t:S],
                                               start=True, stop=True)
                    ins.then_inc(qk2_ready.sem, 1)

                def av2(h):
                    wait(pe, weighted_done, y, h + 1)
                    if h == 0:
                        wait(pe, floor_done, y, 1)
                        wait(pe, ctx_row_in, y, 32)
                        if b is not None:
                            wait(pe, qk_lo_done, b, 2)
                    half, col = h // HALF, VA * (h % HALF)
                    w = weighted[:, h % 3, :]
                    nc.tensor.matmul(ps[:, 4 + 2 * half, col:col + VA], w[:, 0:P], ctx_sb[:, 0, h, :], start=True, stop=True)
                    nc.tensor.matmul(ps[:, 5 + 2 * half, col:col + VA], w[:, P:S], ctx_sb[:, 0, h, :], start=True, stop=False)
                    nc.tensor.matmul(ps[:, 5 + 2 * half, col:col + VA], w[:, S:384], ctx_sb[:, 1, h, :], start=False, stop=True)\
                        .then_inc(av2_head.sem, 1)

                if y is not None:
                    wait(pe, g_rows, y, 1, rest=rest)
                    for t in range(ST):
                        ins = nc.tensor.transpose(ps[:, 4, S + H * t:S + H * t + H], g_log[:, P * t:P * t + P], id_sb[0:H, 0:H])
                    ins.then_inc(glog_ready.sem, 1)
                    for h in range(H):
                        qk2_mm(h)
                        decay_mm(h)
                        if h >= 1:
                            av2(h - 1)
                    av2(H - 1)

                if b is not None:
                    wait(pe, q_in, b, 12 * 16)
                    wait(pe, k_in, b, 12 * 16)
                    if y is not None:
                        wait(pe, weighted_done, y, H)
                    else:
                        wait(pe, rope_done, b, ST)
                    for i in range(PAIRS):
                        if i >= 2:
                            wait(pe, smax_done, b, i - 1)
                        for j in range(2):
                            for t in range(ST):
                                h = 2 * i + j
                                ins = nc.tensor.matmul(ps[:, 2 * (i % 2) + j, S * t:S * t + S], q_stack[0:96, h, P * t:P * t + P],
                                                       k_stack[0:96, h // GQ, :], start=True, stop=True)
                        ins.then_inc(s_ready.sem, 1)
                    wait(pe, smax_done, b, PAIRS)
                    if y is not None:
                        wait(pe, mh_done, y, 2)
                    else:
                        wait(pe, qk_lo_done, b, 2)
                    for t in range(ST):
                        ins = nc.tensor.transpose(ps[0:H, 6, P * t:P * t + P], smax[:, :, t], id_sb[:, :])
                    ins.then_inc(m_ready.sem, 1)

                def t_mm(i):
                    if i == 0:
                        wait(pe, m_in, b, 32)
                    if i >= 2:
                        wait(pe, p_done, b, i - 1)
                    for j in range(2):
                        for t in range(ST):
                            h = 2 * i + j
                            ins = nc.tensor.matmul(ps[:, 2 * (i % 2) + j, S * t:S * t + S], k_stack[0:98, h // GQ, P * t:P * t + P],
                                                   q_stack[0:98, h, :], start=True, stop=True)
                    ins.then_inc(t_ready.sem, 1)

                def av(i):
                    wait(pe, p_done, b, i + 1)
                    if i == 0 and y is not None:
                        wait(pe, x2T_done, y, 1)
                    if i == PAIRS // 2:
                        wait(pe, att_done, b, 1)
                    for j in range(2):
                        h = 2 * i + j
                        col = VA * (h % HALF)
                        for s in range(ST):
                            for t in range(ST):
                                ins = nc.tensor.matmul(ps[:, 4 + s, col:col + VA], probs[:, i % 2, j, t, P * s:P * s + P],
                                                       v_sb[:, t, h // GQ, :], start=t == 0, stop=t == ST - 1)
                    ins.then_inc(av_pair.sem, 1)

                def ug(c):
                    if c >= 2:
                        wait(pe, hT_done, y, c - 1)
                    for w, lo in ((su_sb, 0), (sg_sb, S)):
                        for k in range(KC):
                            ins = nc.tensor.matmul(ps[:, 6 + c % 2, lo:lo + S], w[:, k, P * c:P * c + P], x2T[:, k, :],
                                                   start=k == 0, stop=k == KC - 1)
                    ins.then_inc(ug_ready.sem, 1)

                def down(t):
                    wait(pe, hT_done, y, SC)
                    for c in range(SC):
                        ins = nc.tensor.matmul(ps[:, 2 + t, :], hT[:, c, P * t:P * t + P], sd_sb[:, c, :],
                                               start=c == 0, stop=c == SC - 1)
                    ins.then_inc(sd_ready.sem, 1)

                if b is not None:
                    t_mm(0)
                    t_mm(1)
                if y is not None:
                    wait(pe, x2_done, y, ST)
                    wait(pe, mh_done, y, 2)
                    for c in range(KC):
                        for t in range(ST):
                            ins = nc.tensor.transpose(ps[:, 4 + c // 2, S * (c % 2) + P * t:S * (c % 2) + P * t + P],
                                                      x2[:, t, P * c:P * c + P], id_sb[:, :])
                    ins.then_inc(x2T_ready.sem, 1)
                    wait(pe, x2T_done, y, 1)
                    for t in range(ST):
                        for c in range(KC):
                            ins = nc.tensor.matmul(ps[:, 7, E * t:E * t + E], x2T[:, c, P * t:P * t + P], rw_sb[:, c, :],
                                                   start=c == 0, stop=c == KC - 1)
                    ins.then_inc(lg_ready.sem, 1)
                    if b is not None:
                        wait(pe, m_lo_done, b, 1)
                for c in range(SC):
                    if b is not None and 2 * c + 2 < PAIRS:
                        t_mm(2 * c + 2)
                    if y is not None:
                        if c == 1:
                            wait(pe, lg_done, y, 1)
                        ug(c)
                    if b is not None and c < SC - 1:
                        av(2 * c)
                        t_mm(2 * c + 3)
                        av(2 * c + 1)
                if b is not None:
                    av(PAIRS - 2)
                    av(PAIRS - 1)
                if y is not None:
                    if b is not None:
                        wait(pe, p_done, b, PAIRS)
                    down(0)
                if b is not None:
                    wait(pe, att_done, b, 2)
                    for c in range(KC):
                        for t in range(ST):
                            ins = nc.tensor.transpose(ps[:, 4 + c // 2, S * (c % 2) + P * t:S * (c % 2) + P * t + P],
                                                      att[:, t, P * c:P * c + P], id_sb[:, :])
                    ins.then_inc(attT_ready.sem, 1)
                    wait(pe, attT_done, b, 1)
                    for t in range(ST):
                        for c in range(KC):
                            ins = nc.tensor.matmul(ps[:, t, :], attT[:, c, P * t:P * t + P], wo_sb[:, c, :],
                                                   start=c == 0, stop=c == KC - 1)
                        ins.then_inc(wo_ready.sem, 1)
                if y is not None:
                    down(1)
                if b is not None:
                    wait(pe, x1_done, b, ST)
                    for c in range(KC):
                        for t in range(ST):
                            ins = nc.tensor.transpose(ps[:, 4 + c // 2, S * (c % 2) + P * t:S * (c % 2) + P * t + P],
                                                      x1[:, t, P * c:P * c + P], id_sb[:, :])
                    ins.then_inc(x1T_ready.sem, 1)

            run(pe, body)


def experts(nc, expert_ug, expert_d, ident, before, iota, x2_dram, xs_dram, ys_dram, logits, choice, share, pos_i):
    W = 4
    with ExitStack() as ctx:
        def sb(name, shape, dt=F32):
            return ctx.enter_context(nc.sbuf_tensor(name, shape, dt))

        def sem(name):
            return ctx.enter_context(nc.semaphore(name))

        id_sb = sb("id2_sb", [P, P])
        before_sb = sb("before_sb", [P, P])
        ones_sb = sb("ones_sb", [P, P])
        iota_sb = sb("iota_sb", [P, MT])
        onehot = sb("onehot", [P, TOPK, NT, E])
        chosen = sb("chosen", [P, NT, E])
        totals = sb("totals", [P, E, NT])
        running = sb("running", [P, E, NT])
        ones_t = sb("ones_t", [P, E * NT])
        starts = sb("starts", [P, E])
        counts = sb("counts", [P, E])
        tiles_i = sb("tiles_i", [P, 2, E], I32)
        tiles_f = sb("tiles_f", [P, E])
        tiles_end = sb("tiles_end", [P, E])
        first_row = sb("first_row", [P, E])
        place = sb("place", [P, NT, E])
        product = sb("product", [P, NT, E])
        pos_f = sb("pos_f", [P, TOPK, NT])
        picked = sb("picked", [P, TOPK, NT])
        best = sb("best", [P, NT])
        share_sum = sb("share_sum", [P, NT])
        passed = sb("passed", [1, MT, E])
        owner_f = sb("owner_f", [1, MT])
        owner_i = sb("owner_i", [1, MT], I32)

        x2_all = sb("x2_all", [P, NT, D])
        ug_w = sb("ug_w", [P, W, 2, KC, F])
        d_w = sb("d_w", [P, W, FC, D])
        rows = sb("rows", [P, W, D])
        rowsT = sb("rowsT", [P, 2, KC, P])
        tanh2 = sb("tanh2", [P, 2, FC * P])
        silu2 = sb("silu2", [P, 2, FC * P])
        hidT = sb("hidT", [P, 2, FC, P])
        y_sb = sb("y_sb", [P, 2, D])
        ps = ctx.enter_context(nc.psum_tensor("ps2", [P, 8, 512], F32))

        const_in, x2_in, const_set = sem("const_in"), sem("x2_in"), sem("const_set")
        route_step, chosen_done, prefix_ready = sem("route_step"), sem("chosen_done"), sem("prefix_ready")
        pos_done, owner_done, gap_done, share_exp, share_done = sem("pos_done"), sem("owner_done"), sem("gap_done"), sem("share_exp"), sem("share_done")
        sorted_out = sem("sorted_out")
        ugw_in = [sem(f"ugw_in{s}") for s in range(W)]
        dw_in = [sem(f"dw_in{s}") for s in range(W)]
        rows_in = [sem(f"rows_in{s}") for s in range(W)]
        rowsT_ready, rowsT_done, ug_ready = sem("rowsT_ready"), sem("rowsT_done"), sem("eug_ready")
        tanh_done, silu_done, hid_done = sem("etanh_done"), sem("esilu_done"), sem("ehid_done")
        down_ready, y_done = sem("edown_ready"), sem("ey_done")
        y_out = [sem(f"ey_out{s}") for s in range(2)]

        block = ctx.enter_context(nc.Block())
        xs_v = xs_dram.rearrange("(t p) d -> t p d", p=P)
        ys_v = ys_dram.rearrange("(t p) d -> t p d", p=P)
        x2_v = x2_dram.rearrange("(t p) d -> p t d", p=P)

        def tile_of(v, n):
            return v[n] if isinstance(n, int) else v[bass.ds(n, 1)].rearrange("o p d -> (o p) d")

        def rounds(eng, tile, tail):
            for n in range(W):
                tile(n, n, (n - 1) // 2)
            with eng.Fori(1, MT // W) as r:
                for j in range(W):
                    tile(r * W + j, W + j, r * (W // 2) + (j - 1) // 2)
            tail()


        @block.sync
        def _(sp):
            for dst, src in ((id_sb[:, :], ident), (before_sb[:, :], before), (iota_sb[:, :], iota)):
                sp.dma_start(dst, src).then_inc(const_in, 16)
            for q in range(4):
                part = slice(NT // 4 * q, NT // 4 * (q + 1))
                sp.dma_start(x2_all[:, part, :], x2_v[:, part, :]).then_inc(x2_in, 16)
            sp.wait_ge(owner_done, 1)
            sp.wait_ge(sorted_out, 16 * TOPK * NT)

            def tile(n, k, pairs):
                s = k % W
                owner = sp.value_load(owner_i[0:1, n:n + 1] if isinstance(n, int) else owner_i[0:1, bass.ds(n, 1)],
                                      min_val=0, max_val=E - 1)
                if k >= W:
                    sp.wait_ge(ug_ready, n - W + 1)
                sp.dma_start(ug_w[:, s, :, :, :].rearrange("p g c f -> p (g c f)"),
                             expert_ug[bass.ds(owner, 1)].rearrange("o p n -> (o p) n")).then_inc(ugw_in[s], 16)
                sp.dma_start(rows[:, s, :], tile_of(xs_v, n)).then_inc(rows_in[s], 16)
                if k >= W:
                    sp.wait_ge(down_ready, n - W + 1)
                sp.dma_start(d_w[:, s, :, :].rearrange("p c d -> p (c d)"),
                             expert_d[bass.ds(owner, 1)].rearrange("o p n -> (o p) n")).then_inc(dw_in[s], 16)

            rounds(sp, tile, lambda: None)

        @block.gpsimd
        def _(pool):
            nc.gpsimd.memset(ones_sb[:, :], 1.0).then_inc(const_set, 1)
            nc.gpsimd.memset(ones_t[:, :], 1.0).then_inc(const_set, 1)
            nc.gpsimd.memset(starts[:, :], 0.0).then_inc(const_set, 1)
            pool.wait_ge(x2_in, 16 * 4)
            pool.wait_ge(pos_done, TOPK)
            for t in range(NT):
                for k in range(TOPK):
                    pool.indirect_dma_start(out=xs_dram, out_offset=bass.IndirectOffsetOnAxis(ap=pos_i[:, k, t:t + 1], axis=0),
                                            in_=x2_all[:, t, :], in_offset=None).then_inc(sorted_out, 16)
            pool.wait_ge(sorted_out, 16 * TOPK * NT)

        @block.scalar
        def _(act):
            act.wait_ge(gap_done, TOPK)
            nc.scalar.activation(share[:, :, :], picked[:, :, :], ACT.Exp).then_inc(share_exp, 1)

            def copy_T(n, k):
                act.wait_ge(rowsT_ready, n + 1)
                if k >= 2:
                    act.wait_ge(ug_ready, n - 1)
                nc.scalar.copy(rowsT[:, k % 2, :, :], ps[:, k % 2, :].rearrange("p (c r) -> p c r", r=P)).then_inc(rowsT_done, 1)

            def tile(n, k, pairs):
                copy_T(n, k)
                act.wait_ge(ug_ready, n + 1)
                if k >= 2:
                    act.wait_ge(silu_done, n - 1)
                nc.scalar.activation(tanh2[:, k % 2, :], ps[:, 2 + k % 2, 0:FC * P], ACT.Tanh, scale=0.5).then_inc(tanh_done, 1)
                if k >= 1:
                    act.wait_ge(y_done, n)
                    act.dma_start(tile_of(ys_v, n - 1), y_sb[:, (k - 1) % 2, :]).then_inc(y_out[(k - 1) % 2], 16)

            def tail():
                act.wait_ge(y_done, MT)
                act.dma_start(ys_v[MT - 1], y_sb[:, (MT - 1) % 2, :]).then_inc(y_out[(MT - 1) % 2], 16)
                for s in range(2):
                    act.wait_ge(y_out[s], 16 * (MT // 2))

            rounds(act, tile, tail)

        @block.vector
        def _(dve):
            n_steps = [0]

            def step(ins):
                ins.then_inc(route_step, 1)
                n_steps[0] += 1
                dve.wait_ge(route_step, n_steps[0])

            v = nc.vector
            all3 = [P, NT, E]
            dve.wait_ge(const_in, 3 * 16)
            dve.wait_ge(const_set, 3)
            for k in range(TOPK):
                step(v.tensor_tensor(onehot[:, k, :, :], bcast(choice[:, :, k], all3),
                                     iota_sb[:, 0:E].unsqueeze(1).to_broadcast(all3), ALU.is_equal))
            v.tensor_tensor(chosen[:, :, :], onehot[:, 0, :, :], onehot[:, 1, :, :], ALU.add).then_inc(chosen_done, 1)
            dve.wait_ge(prefix_ready, 1)
            step(v.tensor_copy(totals[:, :, :], ps[:, 1, :].rearrange("p (t e) -> p e t", e=E)))
            run_f = running[:, :, :].rearrange("p e t -> p (e t)")
            step(v.tensor_tensor_scan(run_f, ones_t[:, :], totals[:, :, :].rearrange("p e t -> p (e t)"), 0.0, ALU.mult, ALU.add))
            step(v.tensor_copy(starts[:, 1:E], running[:, 0:E - 1, NT - 1]))
            step(v.tensor_tensor(counts[:, :], running[:, :, NT - 1], starts[:, :], ALU.subtract))
            step(v.tensor_scalar(tiles_i[:, 0, :], counts[:, :], float(P - 1), None, ALU.add))
            step(v.tensor_scalar(tiles_i[:, 1, :], tiles_i[:, 0, :], 7, None, ALU.arith_shift_right))
            step(v.tensor_copy(tiles_f[:, :], tiles_i[:, 1, :]))
            step(v.tensor_tensor_scan(tiles_end[:, :], ones_t[:, 0:E], tiles_f[:, :], 0.0, ALU.mult, ALU.add))
            step(v.tensor_tensor(first_row[:, :], tiles_end[:, :], tiles_f[:, :], ALU.subtract))
            step(v.scalar_tensor_tensor(first_row[:, :], first_row[:, :], float(P), starts[:, :], ALU.mult, ALU.subtract))
            step(v.tensor_tensor(running[:, :, :], running[:, :, :], totals[:, :, :], ALU.subtract))
            step(v.tensor_tensor(running[:, :, :], running[:, :, :], bcast(first_row[:, :], [P, E, NT]), ALU.add))
            step(v.tensor_tensor(place[:, :, :], ps[:, 0, :].rearrange("p (t e) -> p t e", e=E),
                                 running[:, :, :].rearrange("p e t -> p t e"), ALU.add))
            for k in range(TOPK):
                step(v.tensor_tensor(product[:, :, :], onehot[:, k, :, :], place[:, :, :], ALU.mult))
                step(v.tensor_reduce(pos_f[:, k, :], product[:, :, :], AX.X, ALU.add))
                v.tensor_copy(pos_i[:, k, :], pos_f[:, k, :]).then_inc(pos_done, 1)
            shape = [1, MT, E]
            step(v.tensor_tensor(passed[:, :, :], tiles_end[0:1, :].unsqueeze(1).to_broadcast(shape),
                                 bcast(iota_sb[0:1, :], shape), ALU.is_le))
            step(v.tensor_reduce(owner_f[:, :], passed[:, :, :], AX.X, ALU.add))
            v.tensor_scalar(owner_i[:, :], owner_f[:, :], float(E - 1), None, ALU.min).then_inc(owner_done, 1)
            for k in range(TOPK):
                step(v.tensor_tensor(product[:, :, :], onehot[:, k, :, :], logits[:, :, :], ALU.mult))
                step(v.tensor_reduce(picked[:, k, :], product[:, :, :], AX.X, ALU.add))
            step(v.tensor_tensor(best[:, :], picked[:, 0, :], picked[:, 1, :], ALU.max))
            for k in range(TOPK):
                v.tensor_tensor(picked[:, k, :], picked[:, k, :], best[:, :], ALU.subtract).then_inc(gap_done, 1)
            dve.wait_ge(share_exp, 1)
            step(v.tensor_tensor(share_sum[:, :], share[:, 0, :], share[:, 1, :], ALU.add))
            step(v.reciprocal(share_sum[:, :], share_sum[:, :]))
            for k in range(TOPK):
                v.tensor_tensor(share[:, k, :], share[:, k, :], share_sum[:, :], ALU.mult).then_inc(share_done, 1)

            def result(n, k, pairs):
                dve.wait_ge(down_ready, n + 1)
                if k >= 2:
                    dve.wait_ge(y_out[k % 2], 16 * pairs)
                v.tensor_copy(y_sb[:, k % 2, :], ps[:, 4 + k % 2, :]).then_inc(y_done, 1)

            def tile(n, k, pairs):
                dve.wait_ge(tanh_done, n + 1)
                u, g = ps[:, 2 + k % 2, 0:FC * P], ps[:, 2 + k % 2, FC * P:2 * FC * P]
                v.scalar_tensor_tensor(silu2[:, k % 2, :], tanh2[:, k % 2, :], 1.0, u, ALU.add, ALU.mult).then_inc(silu_done, 1)
                dve.wait_ge(silu_done, n + 1)
                if k >= 2:
                    dve.wait_ge(down_ready, n - 1)
                v.scalar_tensor_tensor(hidT[:, k % 2, :, :].rearrange("p c r -> p (c r)"), silu2[:, k % 2, :], 0.5, g,
                                       ALU.mult, ALU.mult).then_inc(hid_done, 1)
                if k >= 1:
                    result(n - 1, k - 1, pairs)

            rounds(dve, tile, lambda: result(MT - 1, MT - 1, (MT - 1) // 2))

        @block.tensor
        def _(pe):
            pe.wait_ge(chosen_done, 1)
            flat = chosen[:, :, :].rearrange("p t e -> p (t e)")
            nc.tensor.matmul(ps[:, 0, :], before_sb[:, :], flat, start=True, stop=True)
            nc.tensor.matmul(ps[:, 1, :], ones_sb[:, :], flat, start=True, stop=True).then_inc(prefix_ready, 1)

            def transpose_rows(k, n, round_end):
                pe.wait_ge(rows_in[k % W], round_end)
                if k >= 2:
                    pe.wait_ge(rowsT_done, n - 1)
                for c in range(KC):
                    ins = nc.tensor.transpose(ps[:, k % 2, P * c:P * c + P], rows[:, k % W, P * c:P * c + P], id_sb[:, :])
                ins.then_inc(rowsT_ready, 1)

            def up(k, n, round_end):
                pe.wait_ge(ugw_in[k % W], round_end)
                pe.wait_ge(rowsT_done, n + 1)
                if k >= 2:
                    pe.wait_ge(hid_done, n - 1)
                for g in range(2):
                    for f in range(FC):
                        col = P * (FC * g + f)
                        for c in range(KC):
                            ins = nc.tensor.matmul(ps[:, 2 + k % 2, col:col + P], ug_w[:, k % W, g, c, P * f:P * f + P],
                                                   rowsT[:, k % 2, c, :], start=c == 0, stop=c == KC - 1)
                ins.then_inc(ug_ready, 1)

            def down(k, n, round_end):
                pe.wait_ge(dw_in[k % W], round_end)
                pe.wait_ge(hid_done, n + 1)
                if k >= 2:
                    pe.wait_ge(y_done, n - 1)
                for f in range(FC):
                    ins = nc.tensor.matmul(ps[:, 4 + k % 2, :], hidT[:, k % 2, f, :], d_w[:, k % W, f, :],
                                           start=f == 0, stop=f == FC - 1)
                ins.then_inc(down_ready, 1)

            pe.wait_ge(pos_done, 1)
            transpose_rows(0, 0, 16)
            for n in range(W):
                up(n, n, 16)
                if n < W - 1:
                    transpose_rows(n + 1, n + 1, 16)
                if n >= 1:
                    down(n - 1, n - 1, 16)
            with pe.Fori(1, MT // W) as r:
                transpose_rows(W, r * W, r * 16 + 16)
                for j in range(W):
                    n = r * W + j
                    up(W + j, n, r * 16 + 16)
                    if j < W - 1:
                        transpose_rows(W + j + 1, n + 1, r * 16 + 16)
                    down(W + j - 1, n - 1, r * 16 + 16 if j else r * 16)
            down(MT - 1, MT - 1, 16 * (MT // W))


def combine(nc, base_dram, ys_dram, share, pos_i, out):
    R = 4
    with ExitStack() as ctx:
        def sb(name, shape, dt=F32):
            return ctx.enter_context(nc.sbuf_tensor(name, shape, dt))

        def sem(name):
            return ctx.enter_context(nc.semaphore(name))

        base = sb("cbase", [P, R, D])
        picked = sb("cpicked", [P, R, TOPK, D])
        total = sb("ctotal", [P, R, D])
        stats = sb("cstats", [P, R, 6])
        mv = sb("cmv", [P, R, 2])
        dev = sb("cdev", [P, R])
        rstd = sb("crstd", [P, R])
        result = sb("cresult", [P, R, D])
        base_in = [sem(f"cbase_in{s}") for s in range(R)]
        picked_in = [sem(f"cpicked_in{s}") for s in range(R)]
        sum_step = Signal(sem("csum_step"), 3)
        added, var_done, dev_done, rstd_done, normed, out_sem = sem("cadded"), sem("cvar"), sem("cdev_s"), sem("crstd_s"), sem("cnormed"), [sem(f"cout{s}") for s in range(R)]
        block = ctx.enter_context(nc.Block())
        base_v = base_dram.rearrange("(t p) d -> t p d", p=P)
        out_v = out.rearrange("b (t p) d -> (b t) p d", p=P)

        def tile_of(v, n):
            return v[n] if isinstance(n, int) else v[bass.ds(n, 1)].rearrange("o p d -> (o p) d")

        def rounds(eng, tile, tail):
            for n in range(2 * R):
                tile(n, n, 16 * (n // R + 1))
            with eng.Fori(2, NT // R) as r:
                for j in range(R):
                    tile(r * R + j, R + j, r * 16 + 16)
            tail()

        @block.sync
        def _(sp):
            def store(n, k):
                sp.wait_ge(normed, n + 1)
                sp.dma_start(tile_of(out_v, n), result[:, k % R, :]).then_inc(out_sem[k % R], 16)

            def tile(n, k, landed):
                if k >= R:
                    sp.wait_ge(added, n - R + 1)
                sp.dma_start(base[:, k % R, :], tile_of(base_v, n)).then_inc(base_in[k % R], 16)
                if k >= 2:
                    store(n - 2, k - 2)

            def tail():
                store(NT - 2, NT - 2)
                store(NT - 1, NT - 1)
                for s in range(R):
                    sp.wait_ge(out_sem[s], 16 * (NT // R))

            rounds(sp, tile, tail)

        @block.gpsimd
        def _(pool):
            for t in range(NT):
                if t >= R:
                    pool.wait_ge(added, t - R + 1)
                for k in range(TOPK):
                    pool.indirect_dma_start(out=picked[:, t % R, k, :], out_offset=None, in_=ys_dram,
                                            in_offset=bass.IndirectOffsetOnAxis(ap=pos_i[:, k, t:t + 1], axis=0))\
                        .then_inc(picked_in[t % R], 16)

        @block.scalar
        def _(act):
            def tile(n, k, landed):
                act.wait_ge(var_done, n + 1)
                if k >= R:
                    act.wait_ge(rstd_done, n - R + 1)
                nc.scalar.activation(dev[:, k % R:k % R + 1], mv[:, k % R, 1:2], ACT.Sqrt).then_inc(dev_done, 1)

            rounds(act, tile, lambda: None)

        @block.vector
        def _(dve):
            v = nc.vector
            rest = (dve.alloc_register("rest2"), base_in[0])

            def finish(n, k, stored):
                s = k % R
                dve.wait_ge(dev_done, n + 1)
                v.reciprocal(rstd[:, s:s + 1], dev[:, s:s + 1]).then_inc(rstd_done, 1)
                dve.wait_ge(rstd_done, n + 1)
                if not isinstance(stored, int) or stored:
                    dve.wait_ge(out_sem[s], stored)
                v.tensor_scalar(result[:, s, :], total[:, s, :], mv[:, s, 0:1], rstd[:, s:s + 1],
                                ALU.subtract, ALU.mult).then_inc(normed, 1)

            def share_of(n, k):
                return share[:, k, n:n + 1] if isinstance(n, int) else share[:, k, bass.ds(n, 1)]

            def tile(n, k, landed):
                s = k % R
                step = Steps(dve, sum_step, n)
                dve.wait_ge(base_in[s], landed)
                dve.wait_ge(picked_in[s], landed * TOPK)
                step(v.scalar_tensor_tensor(total[:, s, :], picked[:, s, 0, :], share_of(n, 0), base[:, s, :], ALU.mult, ALU.add))
                v.scalar_tensor_tensor(total[:, s, :], picked[:, s, 1, :], share_of(n, 1), total[:, s, :], ALU.mult, ALU.add)\
                    .then_inc(added, 1)
                dve.wait_ge(added, n + 1)
                step(v.bn_stats(stats[:, s, :], total[:, s, :]), rest=rest)
                step(v.bn_aggr(mv[:, s, :], stats[:, s, :]))
                step.end()
                v.tensor_scalar(mv[:, s, 1:2], mv[:, s, 1:2], LN_EPS, None, ALU.add).then_inc(var_done, 1)
                if k >= 1:
                    finish(n - 1, k - 1, landed - 16 if k % R else landed - 32)

            rounds(dve, tile, lambda: finish(NT - 1, NT - 1, 16 * (NT // R - 1)))


def _tables():
    inv = (np.float32(1.0) / np.float32(10000.0) ** (np.arange(0, ROT, 2, dtype=np.float32) / np.float32(ROT))).astype(np.float32)
    angle = np.arange(S, dtype=np.float32)[:, None] * inv[None, :]
    cos, sin = np.cos(angle), np.sin(angle)
    cos = np.repeat(cos, 2, axis=1).reshape(ST, P, ROT).transpose(1, 0, 2)
    sin = np.stack([-sin, sin], axis=1).reshape(ST, P, 2, ROT // 2).transpose(1, 0, 2, 3)
    key, query = np.arange(P)[:, None], np.arange(P)[None, :]
    return {
        "rope_cos": cos, "rope_sin": sin, "ident": np.eye(P),
        "mask": np.where(key > query, MASKED, 0.0),
        "before": (key < query) * 1.0,
        "iota": np.broadcast_to(np.arange(MT), (P, MT)),
    }


def kernel(x, ctx_2048, L0_attn_Wq, L0_attn_Wk, L0_attn_Wv, L0_attn_Wo, L0_xattn_Wi, L0_xattn_bi, L0_xattn_Wf,
           L0_xattn_bf, L0_xattn_ln_scale, L0_ffn_router_w, L0_ffn_router_bias, L0_ffn_Wu, L0_ffn_Wg, L0_ffn_Wd,
           L0_ffn_Su, L0_ffn_Sg, L0_ffn_Sd):
    import concourse.bacc as _bacc
    from concourse.bass_utils import run_bass_kernel_spmd as _run

    def chunks(w):
        w = np.asarray(w)
        return w.reshape(-1, P, w.shape[-1]).transpose(1, 0, 2)

    def columns(a):
        return np.asarray(a).transpose(0, 2, 1).reshape(B, KC, P, S).transpose(0, 2, 1, 3)

    def per_expert(w):
        w = np.asarray(w)
        return w.reshape(E, -1, P, w.shape[-1]).transpose(0, 2, 1, 3)

    x, ctx_2048 = np.asarray(x), np.asarray(ctx_2048)
    ins = {
        "x": x.reshape(N, D), "xT": columns(x), "ctx_in": ctx_2048.reshape(N, D), "ctxT": columns(ctx_2048),
        "wqkv": chunks(np.concatenate([np.asarray(L0_attn_Wq), np.asarray(L0_attn_Wk), np.asarray(L0_attn_Wv)], axis=1)),
        "wo": chunks(L0_attn_Wo),
        "gate_w": np.stack([chunks(L0_xattn_Wi), chunks(L0_xattn_Wf)], axis=2),
        "gate_b": np.stack([np.asarray(L0_xattn_bi), np.asarray(L0_xattn_bf)])[:, :, None],
        "ln_scale": np.asarray(L0_xattn_ln_scale), "router_w": chunks(np.asarray(L0_ffn_router_w).T),
        "router_b": np.asarray(L0_ffn_router_bias),
        "expert_ug": np.stack([per_expert(L0_ffn_Wu), per_expert(L0_ffn_Wg)], axis=2).reshape(E, P, -1),
        "expert_d": per_expert(L0_ffn_Wd).reshape(E, P, -1),
        "su": chunks(np.asarray(L0_ffn_Su)[0]), "sg": chunks(np.asarray(L0_ffn_Sg)[0]), "sd": chunks(np.asarray(L0_ffn_Sd)[0]),
    }
    ins.update({k: np.asarray(v, dtype=np.float32) for k, v in _tables().items()})
    nc = _bacc.Bacc("TRN2", target_bir_lowering=False, num_devices=1)
    arrays, args = {}, {}
    for name, a in ins.items():
        a = np.ascontiguousarray(a)
        arrays[f"in_{name}"] = a
        args[name] = nc.dram_tensor(f"in_{name}", a.shape, mybir.dt.from_np(a.dtype), kind="ExternalInput").ap()
    args["out"] = nc.dram_tensor("out_rows", (B, S, D), F32, kind="ExternalOutput").ap()
    decoder_layer(nc, **args)
    r = _run(nc, [arrays], core_ids=[0])
    return r.results[0]["out_rows"]
```
